# Optimizing a Trainium2 kernel written in Bass

```python
import numpy as np
import jax
import jax.numpy as jnp

def _softmax(x, axis=-1):
    return jax.nn.softmax(x, axis=axis)
def _gelu(x):
    return jax.nn.gelu(x, approximate=True)
def _silu(x):
    return jax.nn.silu(x)
def _sigmoid(x):
    return jax.nn.sigmoid(x)
def _layernorm(x, axis=-1, eps=1e-5):
    m = jnp.mean(x, axis=axis, keepdims=True)
    v = jnp.var(x, axis=axis, keepdims=True)
    return (x - m) / jnp.sqrt(v + eps)
def _scatter_add(tgt, idx, src, axis=0):
    return tgt.at[idx].add(src)
def _segment_sum(src, seg, n):
    return jax.ops.segment_sum(src, seg, n)

kernel_name = 'mk_conv_seq_d1_conv_nchw256_4e88a3'

def setup_inputs(seed: int = 0):
    np.random.seed(seed)
    _w = jnp.asarray
    def _rec_inputs():
        import jax
        import jax.numpy as jnp
        _gk = jax.random.key(seed)
        x = -8.015e-05 + 0.9999 * jax.random.normal(jax.random.fold_in(_gk, 1), (32, 256, 80, 80), jnp.float32)
        return x
    x = _rec_inputs()
    def _L0_conv_setup():
        import jax, jax.numpy as jnp
        import numpy as np
        E = 4
        K = 2
        BN_EPS = 0.001

        def _silu(y):
            return y * jax.nn.sigmoid(y)

        def _bn_silu_nchw(y, g, b, m, v):
            scale = (g / jnp.sqrt(v + BN_EPS))[None, :, None, None]
            shift = (b - m * g / jnp.sqrt(v + BN_EPS))[None, :, None, None]
            return _silu(y * scale + shift)
        key = jax.random.key(seed)
        ks = jax.random.split(key, 20)
        B, C1, C2, H, W = (32, 256, 256, 80, 80)
        c_ = C2 // 2
        s = 0.05
        return {'x': jax.random.normal(ks[0], (B, C1, H, W), jnp.float32), 'w1': jax.random.normal(ks[1], (c_, C1), jnp.float32) * s, 'bn1_g': jax.random.uniform(ks[2], (c_,), jnp.float32, 0.5, 1.5), 'bn1_b': jax.random.normal(ks[3], (c_,), jnp.float32) * s, 'bn1_m': jax.random.normal(ks[4], (c_,), jnp.float32) * s, 'bn1_v': jax.random.uniform(ks[5], (c_,), jnp.float32, 0.5, 1.5), 'router_w': jax.random.normal(ks[6], (E, c_), jnp.float32) * s, 'router_b': jax.random.normal(ks[7], (E,), jnp.float32) * s, 'ew': jax.random.normal(ks[8], (E, c_, c_, 3, 3), jnp.float32) * s, 'ebn_g': jax.random.uniform(ks[9], (E, c_), jnp.float32, 0.5, 1.5), 'ebn_b': jax.random.normal(ks[10], (E, c_), jnp.float32) * s, 'ebn_m': jax.random.normal(ks[11], (E, c_), jnp.float32) * s, 'ebn_v': jax.random.uniform(ks[12], (E, c_), jnp.float32, 0.5, 1.5), 'w3': jax.random.normal(ks[13], (C2, c_), jnp.float32) * s, 'bn3_g': jax.random.uniform(ks[14], (C2,), jnp.float32, 0.5, 1.5), 'bn3_b': jax.random.normal(ks[15], (C2,), jnp.float32) * s, 'bn3_m': jax.random.normal(ks[16], (C2,), jnp.float32) * s, 'bn3_v': jax.random.uniform(ks[17], (C2,), jnp.float32, 0.5, 1.5)}
    _L0_conv_all = _L0_conv_setup()
    _L0_conv_in = {k: v for k, v in _L0_conv_all.items() if k in ('w1', 'bn1_g', 'bn1_b', 'bn1_m', 'bn1_v', 'router_w', 'router_b', 'ew', 'ebn_g', 'ebn_b', 'ebn_m', 'ebn_v', 'w3', 'bn3_g', 'bn3_b', 'bn3_m', 'bn3_v', )}
    del _L0_conv_all

    return {
        "x": x,
        "L0_conv_w1": _L0_conv_in["w1"],
        "L0_conv_bn1_g": _L0_conv_in["bn1_g"],
        "L0_conv_bn1_b": _L0_conv_in["bn1_b"],
        "L0_conv_bn1_m": _L0_conv_in["bn1_m"],
        "L0_conv_bn1_v": _L0_conv_in["bn1_v"],
        "L0_conv_router_w": _L0_conv_in["router_w"],
        "L0_conv_router_b": _L0_conv_in["router_b"],
        "L0_conv_ew": _L0_conv_in["ew"],
        "L0_conv_ebn_g": _L0_conv_in["ebn_g"],
        "L0_conv_ebn_b": _L0_conv_in["ebn_b"],
        "L0_conv_ebn_m": _L0_conv_in["ebn_m"],
        "L0_conv_ebn_v": _L0_conv_in["ebn_v"],
        "L0_conv_w3": _L0_conv_in["w3"],
        "L0_conv_bn3_g": _L0_conv_in["bn3_g"],
        "L0_conv_bn3_b": _L0_conv_in["bn3_b"],
        "L0_conv_bn3_m": _L0_conv_in["bn3_m"],
        "L0_conv_bn3_v": _L0_conv_in["bn3_v"],
    }

def reference(x, L0_conv_w1, L0_conv_bn1_g, L0_conv_bn1_b, L0_conv_bn1_m, L0_conv_bn1_v, L0_conv_router_w, L0_conv_router_b, L0_conv_ew, L0_conv_ebn_g, L0_conv_ebn_b, L0_conv_ebn_m, L0_conv_ebn_v, L0_conv_w3, L0_conv_bn3_g, L0_conv_bn3_b, L0_conv_bn3_m, L0_conv_bn3_v):
    import jax
    import jax.numpy as jnp
    def _L0_conv_ref(x, w1, bn1_g, bn1_b, bn1_m, bn1_v, router_w, router_b, ew, ebn_g, ebn_b, ebn_m, ebn_v, w3, bn3_g, bn3_b, bn3_m, bn3_v):
        import jax, jax.numpy as jnp
        import numpy as np
        E = 4
        K = 2
        BN_EPS = 0.001

        def _silu(y):
            return y * jax.nn.sigmoid(y)

        def _bn_silu_nchw(y, g, b, m, v):
            scale = (g / jnp.sqrt(v + BN_EPS))[None, :, None, None]
            shift = (b - m * g / jnp.sqrt(v + BN_EPS))[None, :, None, None]
            return _silu(y * scale + shift)
        B, C1, H, W = x.shape
        c_ = w1.shape[0]
        x_in = _bn_silu_nchw(jnp.einsum('bchw,oc->bohw', x, w1), bn1_g, bn1_b, bn1_m, bn1_v)
        tokens = x_in.transpose(0, 2, 3, 1).reshape(-1, c_)
        N = tokens.shape[0]
        logits = tokens @ router_w.T + router_b
        probs = jax.nn.softmax(logits, axis=-1)
        topw, topi = jax.lax.top_k(probs, K)
        topw = topw / jnp.sum(topw, axis=-1, keepdims=True)
        wd = jnp.zeros((N, E), tokens.dtype).at[jnp.arange(N)[:, None], topi].set(topw)
        center = ew[:, :, :, 1, 1]
        ye = jnp.einsum('nc,eoc->neo', tokens, center)
        inv = ebn_g / jnp.sqrt(ebn_v + BN_EPS)
        ye = _silu(ye * inv[None] + (ebn_b - ebn_m * inv)[None])
        out_moe = jnp.einsum('neo,ne->no', ye, wd)
        out_moe = out_moe.reshape(B, H, W, c_).transpose(0, 3, 1, 2)
        x_out = _bn_silu_nchw(jnp.einsum('bchw,oc->bohw', out_moe, w3), bn3_g, bn3_b, bn3_m, bn3_v)
        return x_out + x

    def _gn(v, G=32, eps=1e-5):
        B_, C_, H_, W_ = v.shape
        g = v.reshape(B_, G, C_ // G, H_, W_)
        m = jnp.mean(g, axis=(2, 3, 4), keepdims=True)
        s = jnp.var(g, axis=(2, 3, 4), keepdims=True)
        return ((g - m) / jnp.sqrt(s + eps)).reshape(v.shape)

    def _ln_c(v, eps=1e-6):
        m = jnp.mean(v, axis=1, keepdims=True)
        s = jnp.var(v, axis=1, keepdims=True)
        return (v - m) / jnp.sqrt(s + eps)

    def _ln_t(v, eps=1e-5):
        m = jnp.mean(v, axis=-1, keepdims=True)
        s = jnp.var(v, axis=-1, keepdims=True)
        return (v - m) / jnp.sqrt(s + eps)

    def _to_tokens(v):
        B_, C_, H_, W_ = v.shape
        return v.reshape(B_, C_, H_ * W_).transpose(0, 2, 1)
    def _from_tokens(t, like):
        B_, C_, H_, W_ = like.shape
        return t.transpose(0, 2, 1).reshape(B_, C_, H_, W_)

    x = _L0_conv_ref(x, L0_conv_w1, L0_conv_bn1_g, L0_conv_bn1_b, L0_conv_bn1_m, L0_conv_bn1_v, L0_conv_router_w, L0_conv_router_b, L0_conv_ew, L0_conv_ebn_g, L0_conv_ebn_b, L0_conv_ebn_m, L0_conv_ebn_v, L0_conv_w3, L0_conv_bn3_g, L0_conv_bn3_b, L0_conv_bn3_m, L0_conv_bn3_v)
    return x


_drawn_inputs = setup_inputs


def setup_inputs(seed=0):
    import zlib

    import numpy as np

    out = dict(_drawn_inputs(seed))
    spreads = {}
    factors = {'L0_conv_bn1_g': 3.337,
     'L0_conv_bn1_b': 8.0,
     'L0_conv_bn1_m': 8.0,
     'L0_conv_bn1_v': 4.463,
     'L0_conv_router_b': 6.003,
     'L0_conv_ebn_g': 4.929,
     'L0_conv_ebn_b': 8.0,
     'L0_conv_ebn_m': 7.935,
     'L0_conv_ebn_v': 8.0,
     'L0_conv_bn3_g': 4.229,
     'L0_conv_bn3_v': 7.827}
    for name, (base, spread) in spreads.items():
        noise = np.random.default_rng([zlib.crc32(name.encode()), seed]).standard_normal(out[name].shape)
        drawn = base * np.exp(spread * noise) if base else spread * noise
        out[name] = jnp.asarray(drawn.astype(out[name].dtype))
    for name, factor in factors.items():
        out[name] = (out[name] * factor).astype(out[name].dtype)
    return out
```

```python
from contextlib import ExitStack
from math import lcm

import concourse.bass as bass
from concourse import mybir

P = 128
F32 = mybir.dt.float32
F32R = mybir.dt.float32r
BF16 = mybir.dt.bfloat16
ACT = mybir.ActivationFunctionType
ALU = mybir.AluOpType
AX_X = mybir.AxisListType.X

BN_EPS = 0.001
CHUNK = 512
BLOCKS = CHUNK // P
PIECE = 640
PERIOD = 10
RING = PERIOD * CHUNK // PIECE
TOK_SLOTS = 5
HEAD = 4
LEAD = 6
LAG = 3
TINY = 1.1754943508222875e-38

MIX_STEPS = 7
MIX_MUL = [1, 2, 4, 5]
MIX_ADD = [None, 3, 6, 7]
MIX_NEEDS = [None, 2, 4, 6]

GATE_TURNS = [["logits", "diff", "beats", "rank", "top", "second_logit", "second"],
              ["gap", "half_sel", "sign", "signed_tanh", "weight", "rest", "low"]]
GATE_OPS = GATE_TURNS[0] + GATE_TURNS[1]
GATE_AT = {name: n + 1 for n, name in enumerate(GATE_OPS)}
PAIRS = PERIOD // 2


def moe_conv_kernel(
    nc: bass.Bass,
    x: bass.AP,
    w1: bass.AP,
    bn1_g: bass.AP,
    bn1_b: bass.AP,
    bn1_m: bass.AP,
    bn1_v: bass.AP,
    router_w: bass.AP,
    router_b: bass.AP,
    ew: bass.AP,
    ebn_g: bass.AP,
    ebn_b: bass.AP,
    ebn_m: bass.AP,
    ebn_v: bass.AP,
    w3: bass.AP,
    bn3_g: bass.AP,
    bn3_b: bass.AP,
    bn3_m: bass.AP,
    bn3_v: bass.AP,
    out: bass.AP,
):
    B, C1, H, W = x.shape
    C = w1.shape[0]
    C2 = w3.shape[0]
    E = router_w.shape[0]
    HW = H * W
    TAPS = ew.shape[3] * ew.shape[4]
    CENTER = TAPS // 2
    KC = C1 // P
    CO = C2 // P
    GATES = BLOCKS * E
    PARTS = 3
    NBN = 1 + E + CO
    n_chunks = B * HW // CHUNK
    n_pieces = B * HW // PIECE
    pieces_per_image = HW // PIECE
    sp_pieces = lcm(RING, pieces_per_image)
    sp_images = sp_pieces // pieces_per_image
    assert C == P and C1 == KC * P and C2 == CO * P and KC == 2 and CO == 2 and E == 4
    assert HW % PIECE == 0 and B * HW % CHUNK == 0 and n_chunks % PERIOD == 0 and n_chunks >= 2 * PERIOD
    assert n_pieces % sp_pieces == 0 and PIECE * RING == CHUNK * PERIOD

    x_v = x.rearrange("b (k p) h w -> b p k (h w)", p=P)
    out_v = out.rearrange("b (k p) h w -> b p k (h w)", p=P)
    ew_v = ew.rearrange("e o c h w -> o e (c h w)")
    w3_v = w3.rearrange("(j p) c -> p j c", p=P)

    ctx = ExitStack()
    with ctx:
        def sb(name, shape, dt=F32):
            return ctx.enter_context(nc.sbuf_tensor(name, shape, dt))

        def sem(name):
            return ctx.enter_context(nc.semaphore(name))

        x_ring = sb("x_ring", [P, KC, RING * PIECE])
        out_ring = sb("out_ring", [P, CO, RING * PIECE])
        x_hi = sb("x_hi", [P, 2, KC, CHUNK], F32R)
        x_lo = sb("x_lo", [P, 2, KC, CHUNK], F32R)
        tok_hi = sb("tok_hi", [P, TOK_SLOTS, CHUNK], F32R)
        tok_lo = sb("tok_lo", [P, TOK_SLOTS, CHUNK], F32R)
        y = sb("y", [P, E, CHUNK])
        acc = sb("acc", [P, E - 1, CHUNK])
        mix_hi = sb("mix_hi", [P, 2, CHUNK], F32R)
        mix_lo = sb("mix_lo", [P, 2, CHUNK], F32R)
        w1_raw = sb("w1_raw", [P, C1])
        w3_raw = sb("w3_raw", [P, CO, C])
        ew_raw = sb("ew_raw", [P, E, C * TAPS])
        rw_raw = sb("rw_raw", [E, C])
        w_scaled = sb("w_scaled", [P, KC + E + CO, P])
        wT_hi = sb("wT_hi", [P, KC + E + CO, P], F32R)
        wT_lo = sb("wT_lo", [P, KC + E + CO, P], F32R)
        router_rhs = sb("router_rhs", [P, 2, E], F32R)
        bn_g = sb("bn_g", [P, NBN])
        bn_b = sb("bn_b", [P, NBN])
        bn_m = sb("bn_m", [P, NBN])
        bn_v = sb("bn_v", [P, NBN])
        bn_root = sb("bn_root", [P, NBN])
        bn_r = sb("bn_r", [P, NBN])
        bn_t = sb("bn_t", [P, NBN])
        bn_scale = sb("bn_scale", [P, NBN])
        shift = sb("shift", [P, NBN])
        rb = sb("rb", [P, E])
        tie = sb("tie", [P, E, E])
        raw_logits = sb("raw_logits", [P, PAIRS, 2, BLOCKS, E])
        G8 = [P, 2 * BLOCKS, E]
        logits = sb("logits", G8)
        diff = sb("diff", [P, 2 * BLOCKS, E, E])
        beats = sb("beats", [P, 2 * BLOCKS, E, E])
        rank = sb("rank", G8)
        top = sb("top", [P, 2 * BLOCKS])
        second_logit = sb("second_logit", G8)
        second = sb("second", [P, 2 * BLOCKS])
        gap = sb("gap", [P, 2 * BLOCKS])
        tanh_gap = sb("tanh_gap", [P, 2 * BLOCKS])
        half_sel = sb("half_sel", G8)
        sign = sb("sign", G8)
        signed_tanh = sb("signed_tanh", G8)
        weight = sb("weight", G8)
        rest = sb("rest", G8)
        gate_parts = sb("gate_parts", [P, 2 * BLOCKS, E, PARTS], BF16)
        gates_T = sb("gates_T", [2 * GATES * PARTS, PAIRS, P], BF16)
        select = sb("select", [2 * GATES * PARTS, 2 * GATES, P], BF16)
        ident = sb("ident", [P, P])
        ident_bf = sb("ident_bf", [P, P], BF16)

        ps_tok = ctx.enter_context(nc.psum_tensor("ps_tok", [P, CHUNK], F32))
        ps_y = ctx.enter_context(nc.psum_tensor("ps_y", [P, 2, CHUNK], F32))
        ps_gate = ctx.enter_context(nc.psum_tensor("ps_gate", [P, 2, CHUNK], F32))
        ps_out = ctx.enter_context(nc.psum_tensor("ps_out", [P, CO, CHUNK], F32))
        ps_misc = ctx.enter_context(nc.psum_tensor("ps_misc", [P, CHUNK], F32))
        ps_logits = ps_misc[:, 0:BLOCKS * 2 * E].rearrange("p (b h e) -> p b h e", b=BLOCKS, h=2)
        ps_gT = ps_misc[0:2 * GATES * PARTS, 256:256 + P // 2].bitcast(BF16)

        params_in = sem("params_in")
        consts_made = sem("consts_made")
        bn_step = sem("bn_step")
        root_made = sem("root_made")
        w_folded = sem("w_folded")
        w_turned = sem("w_turned")
        w_high = sem("w_high")
        w_ready = sem("w_ready")
        x_loaded = [sem(f"x_loaded{n}") for n in range(RING)]
        out_free = [sem(f"out_free{n}") for n in range(RING)]
        x_hi_made = sem("x_hi_made")
        x_lo_made = sem("x_lo_made")
        conv_done = sem("conv_done")
        tok_silu = sem("tok_silu")
        tok_hi_made = sem("tok_hi_made")
        tok_lo_made = sem("tok_lo_made")
        router_done = sem("router_done")
        logits_read = sem("logits_read")
        gate_step = sem("gate_step")
        tanh_made = sem("tanh_made")
        part_made = sem("part_made")
        gate_turned = sem("gate_turned")
        gate_copied = sem("gate_copied")
        expert_done = sem("expert_done")
        y_made = sem("y_made")
        gate_spread = sem("gate_spread")
        mix_step = sem("mix_step")
        mix_hi_made = sem("mix_hi_made")
        mix_lo_made = sem("mix_lo_made")
        out_done = [sem(f"out_done{j}") for j in range(CO)]
        out_silu = [sem(f"out_silu{j}") for j in range(CO)]
        res_added = sem("res_added")

        block = ctx.enter_context(nc.Block())

        def shifted(i, o, n, by):
            return i, o + by, None if n is None else n + by

        def exists(n):
            return n is None or 0 <= n < n_chunks

        def has_before(n, least):
            return n is None or n >= least

        def count(i, o, each=1, plus=0):
            return i * (each * PERIOD) + (each * o + plus)

        def pairs(i, o, each=1, plus=0):
            return i * (each * PAIRS) + (each * (o // 2) + plus)

        def rounds(i, o):
            return i + o // PERIOD

        def pieces_of(o):
            at = o % PERIOD * CHUNK
            return sorted({at // PIECE, (at + CHUNK - 1) // PIECE})

        def place(o):
            at = o % PERIOD * CHUNK
            return slice(at, at + CHUNK)

        def run_steps(engine, step):
            for s in range(-LEAD, HEAD):
                step(0, s, s)
            with engine.Fori(0, n_chunks // PERIOD - 1) as i:
                for u in range(PERIOD):
                    step(i, HEAD + u, None)
            for s in range(n_chunks - PERIOD + HEAD, n_chunks + LAG):
                step(s // PERIOD, s % PERIOD, s)

        @block.sync
        def _(sp):
            with nc.allow_non_contiguous_dma(reason="batch norm parameters, once"):
                for dst, bn1, ebn, bn3 in ((bn_v, bn1_v, ebn_v, bn3_v), (bn_g, bn1_g, ebn_g, bn3_g),
                                           (bn_b, bn1_b, ebn_b, bn3_b), (bn_m, bn1_m, ebn_m, bn3_m)):
                    sp.dma_start(dst[:, 0:1], bn1.rearrange("(p a) -> p a", a=1)).then_inc(params_in, 16)
                    sp.dma_start(dst[:, 1:1 + E], ebn.rearrange("e p -> p e")).then_inc(params_in, 16)
                    sp.dma_start(dst[:, 1 + E:NBN], bn3.rearrange("(j p) -> p j", p=P)).then_inc(params_in, 16)
            sp.dma_start(rb[:, :], router_b.rearrange("(a e) -> a e", a=1).to_broadcast([P, E])).then_inc(params_in, 16)
            sp.dma_start(w1_raw[:, :], w1).then_inc(params_in, 16)
            sp.dma_start(w3_raw[:, :, :], w3_v).then_inc(params_in, 16)
            sp.dma_start(rw_raw[:, :], router_w).then_inc(params_in, 16)
            sp.dma_start(ew_raw[:, :, :], ew_v).then_inc(params_in, 16)
            for n in range(RING):
                sp.sem_inc(out_free[n], 16)

            def load(image, k):
                ring = k % RING * PIECE
                off = k % pieces_per_image * PIECE
                sp.dma_start(x_ring[:, :, ring:ring + PIECE], x_v[image, :, :, off:off + PIECE])\
                    .then_inc(x_loaded[k % RING], 16)

            def store(image, k):
                ring = k % RING * PIECE
                off = k % pieces_per_image * PIECE
                sp.dma_start(out_v[image, :, :, off:off + PIECE], out_ring[:, :, ring:ring + PIECE])\
                    .then_inc(out_free[k % RING], 16)

            def piece(i, k, more):
                last_chunk = -(-(k + 1) * PIECE // CHUNK) - 1
                sp.wait_ge(res_added, i * (sp_pieces * PIECE // CHUNK) + (last_chunk + 1))
                store(i * sp_images + k // pieces_per_image, k)
                if more:
                    load(i * sp_images + (k + RING) // pieces_per_image, k + RING)

            for k in range(RING):
                load(0, k)
            sp_loops = n_pieces // sp_pieces
            if sp_loops > 1:
                with sp.Fori(0, sp_loops - 1) as i:
                    for k in range(sp_pieces):
                        piece(i, k, True)
            for k in range(sp_pieces):
                piece(sp_loops - 1, k, k + RING < sp_pieces)
            for n in range(RING):
                sp.wait_ge(out_free[n], 16 * (n_pieces // RING + 1))

        @block.gpsimd
        def _(pool):
            nc.gpsimd.memset(ident[:, :], 0.0).then_inc(consts_made, 1)
            nc.gpsimd.memset(ident_bf[:, :], 0.0).then_inc(consts_made, 1)
            nc.gpsimd.memset(select[:, :, :], 1.0).then_inc(consts_made, 1)
            nc.gpsimd.memset(tie[:, :, :], -TINY).then_inc(consts_made, 1)
            pool.wait_ge(consts_made, 4)
            for m in (ident, ident_bf):
                nc.gpsimd.affine_select(out=m[:, :], in_=m[:, :], compare_op=ALU.not_equal, fill=1.0, base=0,
                                        pattern=[[-1, P]], channel_multiplier=1).then_inc(consts_made, 1)
            nc.gpsimd.affine_select(out=tie[:, :, :], in_=tie[:, :, :], compare_op=ALU.is_gt, fill=0.0, base=0,
                                    pattern=[[1, E], [-1, E]], channel_multiplier=0).then_inc(consts_made, 1)
            nc.gpsimd.affine_select(out=select[:, :, :], in_=select[:, :, :], compare_op=ALU.is_ge, fill=0.0,
                                    base=0, pattern=[[-PARTS, 2 * GATES], [0, P]], channel_multiplier=1)\
                .then_inc(consts_made, 1)
            pool.wait_ge(consts_made, 8)
            nc.gpsimd.affine_select(out=select[:, :, :], in_=select[:, :, :], compare_op=ALU.is_ge, fill=0.0,
                                    base=PARTS - 1, pattern=[[PARTS, 2 * GATES], [0, P]], channel_multiplier=-1)\
                .then_inc(consts_made, 1)

            def split_x(i, o, n):
                if exists(n):
                    pool.wait_ge(x_hi_made, count(i, o, 1, 1))
                    nc.gpsimd.tensor_tensor(x_lo[:, o % 2], x_ring[:, :, place(o)], x_hi[:, o % 2].bitcast(F32),
                                            ALU.subtract).then_inc(x_lo_made, 1)

            def residual(i, o, n):
                if exists(n):
                    for j in range(CO):
                        pool.wait_ge(out_silu[j], count(i, o, 1, 1))
                    nc.gpsimd.tensor_tensor(out_ring[:, :, place(o)], out_ring[:, :, place(o)],
                                            x_ring[:, :, place(o)], ALU.add).then_inc(res_added, 1)

            def step(i, o, n):
                def at(by):
                    return shifted(i, o, n, by)

                split_x(*at(4))
                residual(*at(-3))

            run_steps(pool, step)

        @block.scalar
        def _(act):
            act.wait_ge(bn_step, 1)
            nc.scalar.activation(bn_root[:, :], bn_t[:, :], ACT.Sqrt).then_inc(root_made, 1)

            def high_x(i, o, n):
                if exists(n):
                    for ring in pieces_of(o):
                        act.wait_ge(x_loaded[ring], rounds(i, o) * 16 + 16)
                    if has_before(n, 2):
                        act.wait_ge(conv_done, count(i, o - 2, 1, 1))
                    nc.scalar.activation(x_hi[:, o % 2], x_ring[:, :, place(o)], ACT.Copy).then_inc(x_hi_made, 1)

            def token_silu(i, o, n):
                if exists(n):
                    act.wait_ge(conv_done, count(i, o, 1, 1))
                    nc.scalar.activation(ps_tok[:, :], ps_tok[:, :], ACT.Silu, bias=shift[:, 0:1]).then_inc(tok_silu, 1)

            def high_tokens(i, o, n):
                if exists(n):
                    act.wait_ge(tok_silu, count(i, o, 1, 1))
                    if has_before(n, TOK_SLOTS):
                        act.wait_ge(expert_done, count(i, o - TOK_SLOTS, E, E))
                    nc.scalar.activation(tok_hi[:, o % TOK_SLOTS], ps_tok[:, :], ACT.Copy).then_inc(tok_hi_made, 1)

            def gap_tanh(i, o, n):
                if exists(n) and o % 2 == 1:
                    act.wait_ge(gate_step, pairs(i, o, len(GATE_OPS), GATE_AT["gap"]))
                    nc.scalar.activation(tanh_gap[:, :], gap[:, :], ACT.Tanh, scale=0.5).then_inc(tanh_made, 1)

            def high_gates(i, o, n):
                if exists(n) and o % 2 == 1:
                    act.wait_ge(gate_step, pairs(i, o, len(GATE_OPS), GATE_AT["weight"]))
                    if has_before(n, 2):
                        act.wait_ge(gate_turned, pairs(i, o))
                    nc.scalar.activation(gate_parts[:, :, :, 0], weight[:, :, :], ACT.Copy).then_inc(part_made, 1)

            def middle_gates(i, o, n):
                if exists(n) and o % 2 == 1:
                    act.wait_ge(gate_step, pairs(i, o, len(GATE_OPS), GATE_AT["rest"]))
                    nc.scalar.activation(gate_parts[:, :, :, 1], rest[:, :, :], ACT.Copy).then_inc(part_made, 1)

            def copy_gates(i, o, n):
                if exists(n) and o % 2 == 0:
                    act.wait_ge(gate_turned, pairs(i, o, 1, 1))
                    nc.scalar.activation(gates_T[:, o // 2 % PAIRS], ps_gT, ACT.Copy).then_inc(gate_copied, 1)

            def expert_silu(i, o, n, e):
                if exists(n):
                    act.wait_ge(expert_done, count(i, o, E, e + 1))
                    if has_before(n, 1):
                        act.wait_ge(mix_step, count(i, o - 1, MIX_STEPS, MIX_MUL[e]))
                    nc.scalar.activation(y[:, e], ps_y[:, e % 2], ACT.Silu, bias=shift[:, 1 + e:2 + e])\
                        .then_inc(y_made, 1)

            def high_mix(i, o, n):
                if exists(n):
                    act.wait_ge(mix_step, count(i, o, MIX_STEPS, MIX_STEPS))
                    if has_before(n, 2):
                        for j in range(CO):
                            act.wait_ge(out_done[j], count(i, o - 2, 1, 1))
                    nc.scalar.activation(mix_hi[:, o % 2], ps_gate[:, 1], ACT.Copy).then_inc(mix_hi_made, 1)

            def output_silu(i, o, n, j):
                if exists(n):
                    act.wait_ge(out_done[j], count(i, o, 1, 1))
                    for ring in pieces_of(o):
                        act.wait_ge(out_free[ring], rounds(i, o) * 16 + 16)
                    nc.scalar.activation(out_ring[:, j, place(o)], ps_out[:, j], ACT.Silu,
                                         bias=shift[:, 1 + E + j:2 + E + j]).then_inc(out_silu[j], 1)

            def step(i, o, n):
                def at(by):
                    return shifted(i, o, n, by)

                output_silu(*at(-2), 0)
                middle_gates(*at(1))
                expert_silu(*at(0), 0)
                copy_gates(*at(0))
                high_mix(*at(-1))
                gap_tanh(*at(2))
                expert_silu(*at(0), 1)
                high_x(*at(5))
                token_silu(*at(4))
                high_gates(*at(2))
                high_tokens(*at(4))
                expert_silu(*at(0), 2)
                expert_silu(*at(0), 3)
                output_silu(*at(-2), 1)

            run_steps(act, step)

        @block.vector
        def _(dve):
            bn_done = 0

            def link(instruction):
                nonlocal bn_done
                bn_done += 1
                instruction.then_inc(bn_step, 1)
                dve.wait_ge(bn_step, bn_done)

            dve.wait_ge(params_in, 16 * 17)
            link(nc.vector.tensor_scalar(bn_t[:, :], bn_v[:, :], BN_EPS, None, ALU.add))
            dve.wait_ge(root_made, 1)
            link(nc.vector.reciprocal(bn_r[:, :], bn_root[:, :]))
            link(nc.vector.tensor_tensor(bn_t[:, :], bn_t[:, :], bn_r[:, :], ALU.mult))
            link(nc.vector.tensor_tensor(bn_t[:, :], bn_t[:, :], bn_r[:, :], ALU.mult))
            link(nc.vector.tensor_scalar(bn_t[:, :], bn_t[:, :], -0.5, 1.5, ALU.mult, ALU.add))
            link(nc.vector.tensor_tensor(bn_r[:, :], bn_r[:, :], bn_t[:, :], ALU.mult))
            link(nc.vector.tensor_tensor(bn_scale[:, :], bn_g[:, :], bn_r[:, :], ALU.mult))
            link(nc.vector.tensor_tensor(bn_t[:, :], bn_m[:, :], bn_scale[:, :], ALU.mult))
            link(nc.vector.tensor_tensor(shift[:, :], bn_b[:, :], bn_t[:, :], ALU.subtract))
            raws = [(w1_raw[:, k * P:(k + 1) * P], 0) for k in range(KC)]
            raws += [(ew_raw[:, e].rearrange("p (c t) -> p c t", t=TAPS)[:, :, CENTER], 1 + e) for e in range(E)]
            raws += [(w3_raw[:, j], 1 + E + j) for j in range(CO)]
            for m, (raw, b) in enumerate(raws):
                nc.vector.tensor_scalar(w_scaled[:, m], raw, bn_scale[:, b:b + 1], None, ALU.mult).then_inc(w_folded, 1)
            for m in range(len(raws) + 1):
                turned = ps_y[:, m % 2, 0:P] if m < len(raws) else ps_y[:, m % 2, 0:E]
                hi = wT_hi[:, m] if m < len(raws) else router_rhs[:, 0]
                lo = wT_lo[:, m] if m < len(raws) else router_rhs[:, 1]
                dve.wait_ge(w_turned, m + 1)
                nc.vector.tensor_copy(hi, turned).then_inc(w_high, 1)
                dve.wait_ge(w_high, m + 1)
                nc.vector.tensor_tensor(lo, turned, hi.bitcast(F32), ALU.subtract).then_inc(w_ready, 1)
            dve.wait_ge(consts_made, 9)

            all_pairs = [P, 2 * BLOCKS, E, E]

            def made(i, o, name):
                return pairs(i, o, len(GATE_OPS), GATE_AT[name])

            def gate(i, o, n, turn):
                if not exists(n):
                    return
                name = GATE_TURNS[o % 2][turn]
                if name == "logits":
                    dve.wait_ge(logits_read, count(i, o + 1, 1, 1))
                    nc.vector.tensor_tensor(
                        logits[:, :, :], raw_logits[:, o // 2 % PAIRS].rearrange("p a b e -> p (a b) e"),
                        rb[:, :].unsqueeze(1).broadcast_to(G8), ALU.add).then_inc(gate_step, 1)
                elif name == "diff":
                    dve.wait_ge(gate_step, made(i, o, "logits"))
                    nc.vector.tensor_tensor(
                        diff[:, :, :, :], logits[:, :, :].unsqueeze(2).broadcast_to(all_pairs),
                        logits[:, :, :].unsqueeze(3).broadcast_to(all_pairs), ALU.subtract).then_inc(gate_step, 1)
                elif name == "beats":
                    dve.wait_ge(gate_step, made(i, o, "diff"))
                    nc.vector.tensor_tensor(
                        beats[:, :, :, :], diff[:, :, :, :], tie[:, :, :].unsqueeze(1).broadcast_to(all_pairs),
                        ALU.is_gt).then_inc(gate_step, 1)
                elif name == "rank":
                    dve.wait_ge(gate_step, made(i, o, "beats"))
                    nc.vector.tensor_reduce(rank[:, :, :], beats[:, :, :, :], AX_X, ALU.add).then_inc(gate_step, 1)
                elif name == "top":
                    dve.wait_ge(gate_step, made(i, o, "logits"))
                    nc.vector.tensor_reduce(top[:, :], logits[:, :, :], AX_X, ALU.max).then_inc(gate_step, 1)
                elif name == "second_logit":
                    dve.wait_ge(gate_step, made(i, o, "rank"))
                    nc.vector.scalar_tensor_tensor(
                        second_logit[:, :, :], rank[:, :, :], 1.0, logits[:, :, :], ALU.is_equal,
                        ALU.mult).then_inc(gate_step, 1)
                elif name == "second":
                    dve.wait_ge(gate_step, made(i, o, "second_logit"))
                    nc.vector.tensor_reduce(second[:, :], second_logit[:, :, :], AX_X, ALU.add).then_inc(gate_step, 1)
                elif name == "gap":
                    dve.wait_ge(gate_step, made(i, o, "second"))
                    nc.vector.tensor_tensor(gap[:, :], top[:, :], second[:, :], ALU.subtract).then_inc(gate_step, 1)
                elif name == "half_sel":
                    dve.wait_ge(gate_step, made(i, o, "rank"))
                    nc.vector.tensor_scalar(half_sel[:, :, :], rank[:, :, :], 2.0, 0.5, ALU.is_lt,
                                            ALU.mult).then_inc(gate_step, 1)
                elif name == "sign":
                    dve.wait_ge(gate_step, made(i, o, "rank"))
                    nc.vector.tensor_scalar(sign[:, :, :], rank[:, :, :], -2.0, 1.0, ALU.mult,
                                            ALU.add).then_inc(gate_step, 1)
                elif name == "signed_tanh":
                    dve.wait_ge(gate_step, made(i, o, "sign"))
                    dve.wait_ge(tanh_made, pairs(i, o, 1, 1))
                    nc.vector.tensor_tensor(
                        signed_tanh[:, :, :], sign[:, :, :], tanh_gap[:, :].unsqueeze(2).broadcast_to(G8),
                        ALU.mult).then_inc(gate_step, 1)
                elif name == "weight":
                    dve.wait_ge(gate_step, made(i, o, "signed_tanh"))
                    nc.vector.scalar_tensor_tensor(
                        weight[:, :, :], signed_tanh[:, :, :], 1.0, half_sel[:, :, :], ALU.add,
                        ALU.mult).then_inc(gate_step, 1)
                elif name == "rest":
                    dve.wait_ge(gate_step, made(i, o, "weight"))
                    dve.wait_ge(part_made, pairs(i, o, 2, 1))
                    nc.vector.tensor_tensor(rest[:, :, :], weight[:, :, :], gate_parts[:, :, :, 0],
                                            ALU.subtract).then_inc(gate_step, 1)
                elif name == "low":
                    dve.wait_ge(gate_step, made(i, o, "rest"))
                    dve.wait_ge(part_made, pairs(i, o, 2, 2))
                    nc.vector.tensor_tensor(gate_parts[:, :, :, 2], rest[:, :, :], gate_parts[:, :, :, 1],
                                            ALU.subtract).then_inc(gate_step, 1)

            def read_logits(i, o, n):
                if exists(n):
                    dve.wait_ge(router_done, count(i, o, 1, 1))
                    nc.vector.tensor_reduce(raw_logits[:, o // 2 % PAIRS, o % 2],
                                            ps_logits.rearrange("p b h e -> p b e h"), AX_X, ALU.add)\
                        .then_inc(logits_read, 1)

            def low_tokens(i, o, n):
                if exists(n):
                    dve.wait_ge(tok_hi_made, count(i, o, 1, 1))
                    nc.vector.tensor_tensor(tok_lo[:, o % TOK_SLOTS], ps_tok[:, :],
                                            tok_hi[:, o % TOK_SLOTS].bitcast(F32), ALU.subtract)\
                        .then_inc(tok_lo_made, 1)

            def mul(i, o, n, e):
                if exists(n):
                    dve.wait_ge(y_made, count(i, o, E, e + 1))
                    dve.wait_ge(gate_spread, count(i, o, E, e + 1))
                    where = acc[:, 0] if e == 0 else ps_gate[:, e % 2]
                    nc.vector.tensor_tensor(where, y[:, e], ps_gate[:, e % 2], ALU.mult).then_inc(mix_step, 1)

            def add(i, o, n, e):
                if exists(n):
                    dve.wait_ge(mix_step, count(i, o, MIX_STEPS, MIX_NEEDS[e]))
                    where = acc[:, e] if e < E - 1 else ps_gate[:, e % 2]
                    nc.vector.tensor_tensor(where, ps_gate[:, e % 2], acc[:, e - 1], ALU.add).then_inc(mix_step, 1)

            def low_mix(i, o, n):
                if exists(n):
                    dve.wait_ge(mix_hi_made, count(i, o, 1, 1))
                    nc.vector.tensor_tensor(mix_lo[:, o % 2], ps_gate[:, 1], mix_hi[:, o % 2].bitcast(F32),
                                            ALU.subtract).then_inc(mix_lo_made, 1)

            def step(i, o, n):
                def at(by):
                    return shifted(i, o, n, by)

                gate(*at(2), 0)
                gate(*at(2), 1)
                gate(*at(2), 2)
                low_mix(*at(-1))
                gate(*at(2), 3)
                mul(*at(0), 0)
                gate(*at(2), 4)
                mul(*at(0), 1)
                add(*at(0), 1)
                low_tokens(*at(4))
                mul(*at(0), 2)
                mul(*at(0), 3)
                gate(*at(2), 5)
                add(*at(0), 2)
                read_logits(*at(4))
                gate(*at(2), 6)
                add(*at(0), 3)

            run_steps(dve, step)

        @block.tensor
        def _(pe):
            pe.wait_ge(consts_made, 9)
            for m in range(KC + E + CO):
                pe.wait_ge(w_folded, m + 1)
                if m >= 2:
                    pe.wait_ge(w_ready, m - 1)
                nc.tensor.transpose(ps_y[:, m % 2, 0:P], w_scaled[:, m], ident[:, :]).then_inc(w_turned, 1)
            m = KC + E + CO
            pe.wait_ge(w_ready, m - 1)
            nc.tensor.transpose(ps_y[:, m % 2, 0:E], rw_raw[:, :], ident[0:E, 0:E]).then_inc(w_turned, 1)
            pe.wait_ge(w_ready, m + 1)

            def product(where, m0, hi, lo):
                terms = []
                for k in range(len(hi)):
                    terms += [(wT_hi[:, m0 + k], hi[k]), (wT_lo[:, m0 + k], hi[k]), (wT_hi[:, m0 + k], lo[k])]
                for t, (w, v) in enumerate(terms):
                    last = nc.tensor.matmul(where, w, v, start=(t == 0), stop=(t == len(terms) - 1))
                return last

            def conv(i, o, n):
                if exists(n):
                    pe.wait_ge(x_lo_made, count(i, o, 1, 1))
                    if has_before(n, 1):
                        pe.wait_ge(tok_lo_made, count(i, o - 1, 1, 1))
                    product(ps_tok[:, :], 0, [x_hi[:, o % 2, k] for k in range(KC)],
                            [x_lo[:, o % 2, k] for k in range(KC)]).then_inc(conv_done, 1)

            def router(i, o, n, turned):
                if exists(n):
                    pe.wait_ge(tok_lo_made, count(i, o, 1, 1))
                    if has_before(n, 1):
                        pe.wait_ge(logits_read, count(i, o - 1, 1, 1))
                    if has_before(turned[2], 0):
                        pe.wait_ge(gate_copied, pairs(turned[0], turned[1], 1, 1))
                    for b in range(BLOCKS):
                        at = slice(b * P, (b + 1) * P)
                        nc.tensor.matmul(ps_logits[:, b].rearrange("p h e -> p (h e)"), tok_hi[:, o % TOK_SLOTS, at],
                                         router_rhs[:, :, :].rearrange("p h e -> p (h e)"), start=True, stop=False)
                        last = nc.tensor.matmul(ps_logits[:, b, 0], tok_lo[:, o % TOK_SLOTS, at],
                                                router_rhs[:, 0], start=False, stop=True)
                    last.then_inc(router_done, 1)

            def turn_gates(i, o, n, routed):
                if exists(n) and o % 2 == 0:
                    pe.wait_ge(gate_step, pairs(i, o, len(GATE_OPS), len(GATE_OPS)))
                    if routed[2] is None or routed[2] < n_chunks:
                        pe.wait_ge(logits_read, count(routed[0], routed[1], 1, 1))
                    nc.tensor.transpose(ps_gT, gate_parts[:, :, :, :].rearrange("p b e t -> p (b e t)"),
                                        ident_bf[:, :]).then_inc(gate_turned, 1)

            def expert(i, o, n, e):
                if exists(n):
                    if e >= 2 or has_before(n, 1):
                        pe.wait_ge(y_made, count(i, o, E, e - 1))
                    product(ps_y[:, e % 2], KC + e, [tok_hi[:, o % TOK_SLOTS]], [tok_lo[:, o % TOK_SLOTS]])\
                        .then_inc(expert_done, 1)

            def spread(i, o, n, e):
                if exists(n):
                    if e == 0:
                        pe.wait_ge(gate_copied, pairs(i, o, 1, 1))
                    if e == 0 and has_before(n, 1):
                        pe.wait_ge(mix_step, count(i, o - 1, MIX_STEPS, MIX_ADD[2]))
                    if e == 1 and has_before(n, 1):
                        pe.wait_ge(mix_lo_made, count(i, o - 1, 1, 1))
                    if e >= 2:
                        pe.wait_ge(mix_step, count(i, o, MIX_STEPS, MIX_MUL[0] if e == 2 else MIX_ADD[1]))
                    for b in range(BLOCKS):
                        last = nc.tensor.matmul(ps_gate[:, e % 2, b * P:(b + 1) * P],
                                                select[:, (o % 2 * BLOCKS + b) * E + e],
                                                gates_T[:, o // 2 % PAIRS], start=True, stop=True)
                    last.then_inc(gate_spread, 1)

            def output(i, o, n, j):
                if exists(n):
                    pe.wait_ge(mix_lo_made, count(i, o, 1, 1))
                    if has_before(n, 1):
                        pe.wait_ge(out_silu[j], count(i, o - 1, 1, 1))
                    product(ps_out[:, j], KC + E + j, [mix_hi[:, o % 2]], [mix_lo[:, o % 2]]).then_inc(out_done[j], 1)

            def step(i, o, n):
                def at(by):
                    return shifted(i, o, n, by)

                expert(*at(0), 0)
                expert(*at(0), 1)
                turn_gates(*at(0), at(3))
                output(*at(-2), 1)
                spread(*at(0), 0)
                conv(*at(4))
                spread(*at(0), 1)
                expert(*at(0), 2)
                expert(*at(0), 3)
                spread(*at(0), 2)
                output(*at(-1), 0)
                spread(*at(0), 3)
                router(*at(4), at(0))

            run_steps(pe, step)


_INS = ["x", "L0_conv_w1", "L0_conv_bn1_g", "L0_conv_bn1_b", "L0_conv_bn1_m", "L0_conv_bn1_v",
        "L0_conv_router_w", "L0_conv_router_b", "L0_conv_ew", "L0_conv_ebn_g", "L0_conv_ebn_b",
        "L0_conv_ebn_m", "L0_conv_ebn_v", "L0_conv_w3", "L0_conv_bn3_g", "L0_conv_bn3_b",
        "L0_conv_bn3_m", "L0_conv_bn3_v"]


def kernel(**inputs):
    import numpy as _np
    import concourse.bacc as _bacc
    from concourse import mybir as _mybir
    from concourse.bass_utils import run_bass_kernel_spmd as _run

    nc = _bacc.Bacc("TRN2", target_bir_lowering=False, num_devices=1)
    arrays, args = {}, []
    for name in _INS:
        a = _np.ascontiguousarray(inputs[name])
        arrays[f"in_{name}_dram"] = a
        args.append(nc.dram_tensor(f"in_{name}_dram", a.shape, _mybir.dt.from_np(a.dtype), kind="ExternalInput").ap())
    shape = inputs["x"].shape
    args.append(nc.dram_tensor("out_0_dram", shape, _mybir.dt.float32, kind="ExternalOutput").ap())
    moe_conv_kernel(nc, *args)
    r = _run(nc, [arrays], core_ids=[0])
    return r.results[0]["out_0_dram"]
```

```python
from contextlib import ExitStack
from math import lcm

import concourse.bass as bass
from concourse import mybir

P = 128
F32 = mybir.dt.float32
F32R = mybir.dt.float32r
BF16 = mybir.dt.bfloat16
ACT = mybir.ActivationFunctionType
ALU = mybir.AluOpType
AX_X = mybir.AxisListType.X

BN_EPS = 0.001
CHUNK = 512
BLOCK = 32
QUARTERS = 4
HALF = CHUNK // 2
BLOCKS = HALF // BLOCK
PIECE = 640
PERIOD = 10
RING = PERIOD * CHUNK // PIECE
TOK_SLOTS = 5
HEAD = 4
LEAD = 6
LAG = 3
LATE_WEIGHTS_AT = -2
EARLY_PIECES = 3
TINY = 1.1754943508222875e-38

MIX_STEPS = 7
MIX_MUL = [1, 2, 4, 6]
MIX_ADD = [None, 3, 5, 7]
MIX_NEEDS = [None, 2, 4, 6]

GATE_TURNS = [["turned_logits", "diff", "beats", "rank", "top", "second_logit"],
              ["second", "gap", "weight", "rest", "low", "turned_gates"]]
GATE_OPS = GATE_TURNS[0] + GATE_TURNS[1]
GATE_AT = {name: n + 1 for n, name in enumerate(GATE_OPS)}
SIDE_TURNS = [["part_sum", "logits"], ["signed_tanh", "half_more"]]
SIDE_OPS = SIDE_TURNS[0] + SIDE_TURNS[1]
SIDE_AT = {name: n + 1 for n, name in enumerate(SIDE_OPS)}
PAIRS = PERIOD // 2


def moe_conv_kernel(
    nc: bass.Bass,
    x: bass.AP,
    w1: bass.AP,
    bn1_g: bass.AP,
    bn1_b: bass.AP,
    bn1_m: bass.AP,
    bn1_v: bass.AP,
    router_w: bass.AP,
    router_b: bass.AP,
    ew: bass.AP,
    ebn_g: bass.AP,
    ebn_b: bass.AP,
    ebn_m: bass.AP,
    ebn_v: bass.AP,
    w3: bass.AP,
    bn3_g: bass.AP,
    bn3_b: bass.AP,
    bn3_m: bass.AP,
    bn3_v: bass.AP,
    out: bass.AP,
):
    B, C1, H, W = x.shape
    C = w1.shape[0]
    C2 = w3.shape[0]
    E = router_w.shape[0]
    HW = H * W
    TAPS = ew.shape[3] * ew.shape[4]
    CENTER = TAPS // 2
    KC = C1 // P
    CO = C2 // P
    PARTS = 3
    NBN = 1 + E + CO
    n_chunks = B * HW // CHUNK
    n_pieces = B * HW // PIECE
    pieces_per_image = HW // PIECE
    sp_pieces = lcm(RING, pieces_per_image)
    sp_images = sp_pieces // pieces_per_image
    assert C == P and C1 == KC * P and C2 == CO * P and KC == 2 and CO == 2 and E == 4
    assert HW % PIECE == 0 and B * HW % CHUNK == 0 and n_chunks % PERIOD == 0 and n_chunks >= 2 * PERIOD
    assert n_pieces % sp_pieces == 0 and PIECE * RING == CHUNK * PERIOD

    x_v = x.rearrange("b (k p) h w -> b p k (h w)", p=P)
    out_v = out.rearrange("b (k p) h w -> b p k (h w)", p=P)
    ew_v = ew.rearrange("e o c h w -> o e (c h w)")
    w3_v = w3.rearrange("(j p) c -> p j c", p=P)

    ctx = ExitStack()
    with ctx:
        def sb(name, shape, dt=F32):
            return ctx.enter_context(nc.sbuf_tensor(name, shape, dt))

        def sem(name):
            return ctx.enter_context(nc.semaphore(name))

        x_ring = sb("x_ring", [P, KC, RING * PIECE])
        out_ring = sb("out_ring", [P, CO, RING * PIECE])
        x_hi = sb("x_hi", [P, 2, KC, CHUNK], F32R)
        x_lo = sb("x_lo", [P, 2, KC, CHUNK], F32R)
        tok_hi = sb("tok_hi", [P, TOK_SLOTS, CHUNK], F32R)
        tok_lo = sb("tok_lo", [P, TOK_SLOTS, CHUNK], F32R)
        y = sb("y", [P, E, CHUNK])
        acc = sb("acc", [P, E - 1, CHUNK])
        mix_hi = sb("mix_hi", [P, 2, CHUNK], F32R)
        mix_lo = sb("mix_lo", [P, 2, CHUNK], F32R)
        w1_raw = sb("w1_raw", [P, C1])
        w3_raw = sb("w3_raw", [P, CO, C])
        ew_raw = sb("ew_raw", [P, E, C * TAPS])
        rw_raw = sb("rw_raw", [E, C])
        w_scaled = sb("w_scaled", [P, KC + E + CO, P])
        wT_hi = sb("wT_hi", [P, KC + E + CO, P], F32R)
        wT_lo = sb("wT_lo", [P, KC + E + CO, P], F32R)
        router_both = sb("router_both", [P, QUARTERS * (P + BLOCK)], F32R)
        router_hi = sb("router_hi", [P, QUARTERS * (P + BLOCK)], F32R)
        bn_g = sb("bn_g", [P, NBN])
        bn_b = sb("bn_b", [P, NBN])
        bn_m = sb("bn_m", [P, NBN])
        bn_v = sb("bn_v", [P, NBN])
        bn_root = sb("bn_root", [P, NBN])
        bn_r = sb("bn_r", [P, NBN])
        bn_t = sb("bn_t", [P, NBN])
        bn_scale = sb("bn_scale", [P, NBN])
        shift = sb("shift", [P, NBN])
        rb = sb("rb", [P, E])
        tie = sb("tie", [P, E, E])
        turned_logits = sb("turned_logits", [P, BLOCKS, BLOCK])
        G8 = [P, BLOCKS, E]
        part_sum = sb("part_sum", G8)
        logits = sb("logits", G8)
        top = sb("top", [P, BLOCKS])
        second_logit = sb("second_logit", G8)
        gap = sb("gap", [P, BLOCKS])
        tanh_gap = sb("tanh_gap", [P, BLOCKS])
        half_sign = sb("half_sign", G8)
        half_more = sb("half_more", G8)
        half = sb("half", [P, 1])
        signed_tanh = sb("signed_tanh", G8)
        gate_parts = sb("gate_parts", [P, BLOCKS, BLOCK], BF16)
        gates_T = sb("gates_T", [P, PAIRS, HALF], BF16)
        select = sb("select", [P, QUARTERS * E, P], BF16)
        ident = sb("ident", [P, P])

        ps_tok = ctx.enter_context(nc.psum_tensor("ps_tok", [P, CHUNK], F32))
        ps_y = ctx.enter_context(nc.psum_tensor("ps_y", [P, 2, CHUNK], F32))
        ps_gate = ctx.enter_context(nc.psum_tensor("ps_gate", [P, 2, CHUNK], F32))
        ps_out = ctx.enter_context(nc.psum_tensor("ps_out", [P, CHUNK], F32))
        ps_logits = ctx.enter_context(nc.psum_tensor("ps_logits", [P, CHUNK], F32))
        ps_gating = ctx.enter_context(nc.psum_tensor("ps_gating", [P, CHUNK], F32))

        GW = BLOCKS * E
        logits_copy, rank, weight, rest = (
            ps_gating[:, k * GW:(k + 1) * GW].rearrange("p (b e) -> p b e", e=E) for k in range(4))
        diff, beats = (
            ps_gating[:, k * GW:(k + E) * GW].rearrange("p (b e f) -> p b e f", e=E, f=E) for k in (4, 4 + E))
        second = ps_gating[:, (4 + 2 * E) * GW:(4 + 2 * E) * GW + BLOCKS]

        both_hi = router_both[:, :].rearrange("p (q c) -> p q c", q=QUARTERS)[:, :, 0:E]
        both_lo = router_both[:, :].rearrange("p (q c) -> p q c", q=QUARTERS)[:, :, E:2 * E]
        hi_alone = router_hi[:, :].rearrange("p (q c) -> p q c", q=QUARTERS)[:, :, 0:E]
        parts = gate_parts[:, :, 0:E * PARTS].rearrange("p b (e t) -> p b e t", t=PARTS)

        params_in = sem("params_in")
        late_weights_in = sem("late_weights_in")
        consts_made = sem("consts_made")
        bn_step = sem("bn_step")
        root_made = sem("root_made")
        w_folded = sem("w_folded")
        w_turned = sem("w_turned")
        w_high = sem("w_high")
        w_ready = sem("w_ready")
        x_loaded = [sem(f"x_loaded{n}") for n in range(RING)]
        out_free = [sem(f"out_free{n}") for n in range(RING)]
        x_hi_made = sem("x_hi_made")
        x_lo_made = sem("x_lo_made")
        conv_done = sem("conv_done")
        tok_silu = sem("tok_silu")
        tok_hi_made = sem("tok_hi_made")
        tok_lo_made = sem("tok_lo_made")
        router_done = sem("router_done")
        gate_step = sem("gate_step")
        tanh_made = sem("tanh_made")
        part_made = sem("part_made")
        logits_copied = sem("logits_copied")
        sign_made = sem("sign_made")
        side_step = sem("side_step")
        expert_done = sem("expert_done")
        y_made = sem("y_made")
        gate_spread = sem("gate_spread")
        mix_step = sem("mix_step")
        mix_hi_made = sem("mix_hi_made")
        mix_lo_made = sem("mix_lo_made")
        out_done = [sem(f"out_done{j}") for j in range(CO)]
        out_silu = [sem(f"out_silu{j}") for j in range(CO)]
        res_added = sem("res_added")

        block = ctx.enter_context(nc.Block())

        PARAMS = 3 * 4 + 3
        ROUTER_TURN = KC
        HIGHS_AT = [t + (t > ROUTER_TURN) for t in range(KC + 1 + E + CO)]

        def shifted(i, o, n, by):
            return i, o + by, None if n is None else n + by

        def exists(n):
            return n is None or 0 <= n < n_chunks

        def has_before(n, least):
            return n is None or n >= least

        def count(i, o, each=1, plus=0):
            return i * (each * PERIOD) + (each * o + plus)

        def pairs(i, o, each=1, plus=0):
            return i * (each * PAIRS) + (each * (o // 2) + plus)

        def made(i, o, name):
            return pairs(i, o, len(GATE_OPS), GATE_AT[name])

        def side_made(i, o, name):
            return pairs(i, o, len(SIDE_OPS), SIDE_AT[name])

        def bank(o, e):
            return 1 - o % 2 if e == 2 else o % 2

        def rounds(i, o):
            return i + o // PERIOD

        def pieces_of(o):
            at = o % PERIOD * CHUNK
            return sorted({at // PIECE, (at + CHUNK - 1) // PIECE})

        def place(o):
            at = o % PERIOD * CHUNK
            return slice(at, at + CHUNK)

        def run_steps(engine, step, lead_in):
            for s in range(-LEAD, 0):
                lead_in(0, s, s)
            for s in range(HEAD):
                step(0, s, s)
            with engine.Fori(0, n_chunks // PERIOD - 1) as i:
                for u in range(PERIOD):
                    step(i, HEAD + u, None)
            for s in range(n_chunks - PERIOD + HEAD, n_chunks + LAG):
                step(s // PERIOD, s % PERIOD, s)

        @block.sync
        def _(sp):
            def load(image, k):
                ring = k % RING * PIECE
                off = k % pieces_per_image * PIECE
                sp.dma_start(x_ring[:, :, ring:ring + PIECE], x_v[image, :, :, off:off + PIECE])\
                    .then_inc(x_loaded[k % RING], 16)

            load(0, 0)
            with nc.allow_non_contiguous_dma(reason="batch norm parameters, once"):
                for dst, bn1, ebn, bn3 in ((bn_v, bn1_v, ebn_v, bn3_v), (bn_g, bn1_g, ebn_g, bn3_g),
                                           (bn_b, bn1_b, ebn_b, bn3_b), (bn_m, bn1_m, ebn_m, bn3_m)):
                    sp.dma_start(dst[:, 0:1], bn1.rearrange("(p a) -> p a", a=1)).then_inc(params_in, 16)
                    sp.dma_start(dst[:, 1:1 + E], ebn.rearrange("e p -> p e")).then_inc(params_in, 16)
                    sp.dma_start(dst[:, 1 + E:NBN], bn3.rearrange("(j p) -> p j", p=P)).then_inc(params_in, 16)
            sp.dma_start(rb[:, :], router_b.rearrange("(a e) -> a e", a=1).to_broadcast([P, E])).then_inc(params_in, 16)
            sp.dma_start(w1_raw[:, :], w1).then_inc(params_in, 16)
            sp.dma_start(rw_raw[:, :], router_w).then_inc(params_in, 16)
            for n in range(RING):
                sp.sem_inc(out_free[n], 16)

            def store(image, k):
                ring = k % RING * PIECE
                off = k % pieces_per_image * PIECE
                sp.dma_start(out_v[image, :, :, off:off + PIECE], out_ring[:, :, ring:ring + PIECE])\
                    .then_inc(out_free[k % RING], 16)

            def piece(i, k, more):
                last_chunk = -(-(k + 1) * PIECE // CHUNK) - 1
                sp.wait_ge(res_added, i * (sp_pieces * PIECE // CHUNK) + (last_chunk + 1))
                store(i * sp_images + k // pieces_per_image, k)
                if more:
                    load(i * sp_images + (k + RING) // pieces_per_image, k + RING)

            for k in range(1, RING):
                if k == EARLY_PIECES:
                    sp.dma_start(ew_raw[:, :, :], ew_v).then_inc(late_weights_in, 16)
                    sp.dma_start(w3_raw[:, :, :], w3_v).then_inc(late_weights_in, 16)
                load(0, k)
            sp_loops = n_pieces // sp_pieces
            if sp_loops > 1:
                with sp.Fori(0, sp_loops - 1) as i:
                    for k in range(sp_pieces):
                        piece(i, k, True)
            for k in range(sp_pieces):
                piece(sp_loops - 1, k, k + RING < sp_pieces)
            for n in range(RING):
                sp.wait_ge(out_free[n], 16 * (n_pieces // RING + 1))

        @block.gpsimd
        def _(pool):
            nc.gpsimd.memset(ident[:, :], 0.0).then_inc(consts_made, 1)
            nc.gpsimd.memset(select[:, :, :], 1.0).then_inc(consts_made, 1)
            nc.gpsimd.memset(half[:, :], 0.5).then_inc(consts_made, 1)
            nc.gpsimd.memset(tie[:, :, :], -TINY).then_inc(consts_made, 1)
            nc.gpsimd.memset(gate_parts[:, :, :], 0.0).then_inc(consts_made, 1)
            nc.gpsimd.memset(router_both[:, :].bitcast(F32), 0.0).then_inc(consts_made, 1)
            nc.gpsimd.memset(router_hi[:, :].bitcast(F32), 0.0).then_inc(consts_made, 1)
            pool.wait_ge(consts_made, 7)
            nc.gpsimd.affine_select(out=ident[:, :], in_=ident[:, :], compare_op=ALU.not_equal, fill=1.0, base=0,
                                    pattern=[[-1, P]], channel_multiplier=1).then_inc(consts_made, 1)
            nc.gpsimd.affine_select(out=tie[:, :, :], in_=tie[:, :, :], compare_op=ALU.is_gt, fill=0.0, base=0,
                                    pattern=[[1, E], [-1, E]], channel_multiplier=0).then_inc(consts_made, 1)
            for_parts = select[:, :, :].rearrange("p (q e) m -> p q e m", q=QUARTERS)
            nc.gpsimd.affine_select(out=for_parts, in_=for_parts, compare_op=ALU.is_ge, fill=0.0, base=0,
                                    pattern=[[-BLOCK, QUARTERS], [-PARTS, E], [0, P]], channel_multiplier=1)\
                .then_inc(consts_made, 1)
            pool.wait_ge(consts_made, 10)
            nc.gpsimd.affine_select(out=for_parts, in_=for_parts, compare_op=ALU.is_ge, fill=0.0, base=PARTS - 1,
                                    pattern=[[BLOCK, QUARTERS], [PARTS, E], [0, P]], channel_multiplier=-1)\
                .then_inc(consts_made, 1)

            def side_gate(i, o, n, turn):
                if not exists(n) or turn >= len(SIDE_TURNS[o % 2]):
                    return
                name = SIDE_TURNS[o % 2][turn]
                if name == "part_sum":
                    pool.wait_ge(gate_step, made(i, o, "turned_logits"))
                    nc.gpsimd.tensor_tensor(part_sum[:, :, :], turned_logits[:, :, 0:E],
                                            turned_logits[:, :, E:2 * E], ALU.add).then_inc(side_step, 1)
                elif name == "logits":
                    pool.wait_ge(side_step, side_made(i, o, "part_sum"))
                    nc.gpsimd.tensor_tensor(logits[:, :, :], part_sum[:, :, :],
                                            rb[:, :].unsqueeze(1).broadcast_to(G8), ALU.add).then_inc(side_step, 1)
                elif name == "signed_tanh":
                    pool.wait_ge(sign_made, pairs(i, o, 1, 1))
                    pool.wait_ge(tanh_made, pairs(i, o, 1, 1))
                    nc.gpsimd.tensor_tensor(signed_tanh[:, :, :], half_sign[:, :, :],
                                            tanh_gap[:, :].unsqueeze(2).broadcast_to(G8), ALU.mult)\
                        .then_inc(side_step, 1)
                elif name == "half_more":
                    pool.wait_ge(side_step, side_made(i, o, "signed_tanh"))
                    nc.gpsimd.tensor_tensor(half_more[:, :, :], signed_tanh[:, :, :],
                                            half[:, :].unsqueeze(2).broadcast_to(G8), ALU.add).then_inc(side_step, 1)

            def split_x(i, o, n):
                if exists(n):
                    pool.wait_ge(x_hi_made, count(i, o, 1, 1))
                    nc.gpsimd.tensor_tensor(x_lo[:, o % 2], x_ring[:, :, place(o)], x_hi[:, o % 2].bitcast(F32),
                                            ALU.subtract).then_inc(x_lo_made, 1)

            def residual(i, o, n):
                if exists(n):
                    for j in range(CO):
                        pool.wait_ge(out_silu[j], count(i, o, 1, 1))
                    nc.gpsimd.tensor_tensor(out_ring[:, :, place(o)], out_ring[:, :, place(o)],
                                            x_ring[:, :, place(o)], ALU.add).then_inc(res_added, 1)

            def lead_in(i, o, n):
                def at(by):
                    return shifted(i, o, n, by)

                side_gate(*at(2), 0)
                side_gate(*at(2), 1)
                split_x(*at(5))

            def step(i, o, n):
                def at(by):
                    return shifted(i, o, n, by)

                side_gate(*at(2), 0)
                side_gate(*at(2), 1)
                residual(*at(-2))
                split_x(*at(5))

            run_steps(pool, step, lead_in)

        @block.scalar
        def _(act):
            act.wait_ge(bn_step, 1)
            nc.scalar.activation(bn_root[:, :], bn_t[:, :], ACT.Sqrt).then_inc(root_made, 1)

            def high_x(i, o, n):
                if exists(n):
                    for ring in pieces_of(o):
                        act.wait_ge(x_loaded[ring], rounds(i, o) * 16 + 16)
                    if has_before(n, 2):
                        act.wait_ge(conv_done, count(i, o - 2, 1, 1))
                    nc.scalar.activation(x_hi[:, o % 2], x_ring[:, :, place(o)], ACT.Copy).then_inc(x_hi_made, 1)

            def token_silu(i, o, n):
                if exists(n):
                    act.wait_ge(conv_done, count(i, o, 1, 1))
                    nc.scalar.activation(ps_tok[:, :], ps_tok[:, :], ACT.Silu, bias=shift[:, 0:1]).then_inc(tok_silu, 1)

            def high_tokens(i, o, n):
                if exists(n):
                    act.wait_ge(tok_silu, count(i, o, 1, 1))
                    if has_before(n, TOK_SLOTS):
                        act.wait_ge(expert_done, count(i, o - TOK_SLOTS, E, E))
                    nc.scalar.activation(tok_hi[:, o % TOK_SLOTS], ps_tok[:, :], ACT.Copy).then_inc(tok_hi_made, 1)

            def copy_logits(i, o, n):
                if exists(n) and o % 2 == 0:
                    act.wait_ge(side_step, side_made(i, o, "logits"))
                    if has_before(n, 2):
                        act.wait_ge(gate_step, made(i, o - 2, "low"))
                    nc.scalar.activation(logits_copy, logits[:, :, :], ACT.Copy).then_inc(logits_copied, 1)

            def signs(i, o, n):
                if exists(n) and o % 2 == 0:
                    act.wait_ge(gate_step, made(i, o, "rank"))
                    nc.scalar.activation(half_sign[:, :, :], rank, ACT.Copy, bias=0.5, scale=-1.0)\
                        .then_inc(sign_made, 1)

            def gap_tanh(i, o, n):
                if exists(n) and o % 2 == 1:
                    act.wait_ge(gate_step, made(i, o, "gap"))
                    nc.scalar.activation(tanh_gap[:, :], gap[:, :], ACT.Tanh, scale=0.5).then_inc(tanh_made, 1)

            def high_gates(i, o, n):
                if exists(n) and o % 2 == 1:
                    act.wait_ge(gate_step, made(i, o, "weight"))
                    nc.scalar.activation(parts[:, :, :, 0], weight, ACT.Copy).then_inc(part_made, 1)

            def middle_gates(i, o, n):
                if exists(n) and o % 2 == 1:
                    act.wait_ge(gate_step, made(i, o, "rest"))
                    nc.scalar.activation(parts[:, :, :, 1], rest, ACT.Copy).then_inc(part_made, 1)

            def expert_silu(i, o, n, e):
                if exists(n):
                    act.wait_ge(expert_done, count(i, o, E, e + 1))
                    if has_before(n, 1):
                        act.wait_ge(mix_step, count(i, o - 1, MIX_STEPS, MIX_MUL[e]))
                    nc.scalar.activation(y[:, e], ps_y[:, e % 2], ACT.Silu, bias=shift[:, 1 + e:2 + e])\
                        .then_inc(y_made, 1)

            def high_mix(i, o, n):
                if exists(n):
                    act.wait_ge(mix_step, count(i, o, MIX_STEPS, MIX_STEPS))
                    if has_before(n, 2):
                        for j in range(CO):
                            act.wait_ge(out_done[j], count(i, o - 2, 1, 1))
                    nc.scalar.activation(mix_hi[:, o % 2], ps_gate[:, bank(o, E - 1)], ACT.Copy).then_inc(mix_hi_made, 1)

            def output_silu(i, o, n, j):
                if exists(n):
                    act.wait_ge(out_done[j], count(i, o, 1, 1))
                    for ring in pieces_of(o):
                        act.wait_ge(out_free[ring], rounds(i, o) * 16 + 16)
                    nc.scalar.activation(out_ring[:, j, place(o)], ps_out[:, :], ACT.Silu,
                                         bias=shift[:, 1 + E + j:2 + E + j]).then_inc(out_silu[j], 1)

            def lead_in(i, o, n):
                def at(by):
                    return shifted(i, o, n, by)

                high_x(*at(5))
                copy_logits(*at(2))
                gap_tanh(*at(2))
                high_gates(*at(2))
                token_silu(*at(4))
                middle_gates(*at(2))
                high_tokens(*at(4))
                signs(*at(2))

            def step(i, o, n):
                def at(by):
                    return shifted(i, o, n, by)

                expert_silu(*at(0), 0)
                expert_silu(*at(0), 1)
                output_silu(*at(-2), 0)
                high_mix(*at(-1))
                high_x(*at(5))
                copy_logits(*at(2))
                expert_silu(*at(0), 2)
                gap_tanh(*at(2))
                output_silu(*at(-2), 1)
                expert_silu(*at(0), 3)
                high_gates(*at(2))
                token_silu(*at(4))
                middle_gates(*at(2))
                high_tokens(*at(4))
                signs(*at(2))

            run_steps(act, step, lead_in)

        @block.vector
        def _(dve):
            bn_done = 0

            def link(instruction):
                nonlocal bn_done
                bn_done += 1
                instruction.then_inc(bn_step, 1)
                dve.wait_ge(bn_step, bn_done)

            dve.wait_ge(params_in, 16 * PARAMS)
            link(nc.vector.tensor_scalar(bn_t[:, :], bn_v[:, :], BN_EPS, None, ALU.add))
            dve.wait_ge(root_made, 1)
            link(nc.vector.reciprocal(bn_r[:, :], bn_root[:, :]))
            link(nc.vector.tensor_tensor(bn_t[:, :], bn_t[:, :], bn_r[:, :], ALU.mult))
            link(nc.vector.tensor_tensor(bn_t[:, :], bn_t[:, :], bn_r[:, :], ALU.mult))
            link(nc.vector.tensor_scalar(bn_t[:, :], bn_t[:, :], -0.5, 1.5, ALU.mult, ALU.add))
            link(nc.vector.tensor_tensor(bn_r[:, :], bn_r[:, :], bn_t[:, :], ALU.mult))
            link(nc.vector.tensor_tensor(bn_scale[:, :], bn_g[:, :], bn_r[:, :], ALU.mult))
            link(nc.vector.tensor_tensor(bn_t[:, :], bn_m[:, :], bn_scale[:, :], ALU.mult))
            link(nc.vector.tensor_tensor(shift[:, :], bn_b[:, :], bn_t[:, :], ALU.subtract))
            def fold(m, raw, b):
                nc.vector.tensor_scalar(w_scaled[:, m], raw, bn_scale[:, b:b + 1], None, ALU.mult).then_inc(w_folded, 1)

            def split_weights(t, m):
                turned = ps_y[:, t % 2, 0:P]
                dve.wait_ge(w_turned, t + 1)
                nc.vector.tensor_copy(wT_hi[:, m], turned).then_inc(w_high, 1)
                dve.wait_ge(w_high, HIGHS_AT[t] + 1)
                nc.vector.tensor_tensor(wT_lo[:, m], turned, wT_hi[:, m].bitcast(F32), ALU.subtract)\
                    .then_inc(w_ready, 1)

            for k in range(KC):
                fold(k, w1_raw[:, k * P:(k + 1) * P], 0)
            for k in range(KC):
                split_weights(k, k)
            t = ROUTER_TURN
            turned = ps_y[:, t % 2, 0:E].unsqueeze(1).broadcast_to([P, QUARTERS, E])
            dve.wait_ge(consts_made, 11)
            dve.wait_ge(w_turned, t + 1)
            nc.vector.tensor_copy(both_hi, turned).then_inc(w_high, 1)
            nc.vector.tensor_copy(hi_alone, turned).then_inc(w_high, 1)
            dve.wait_ge(w_high, HIGHS_AT[t] + 2)
            nc.vector.tensor_tensor(both_lo, turned, both_hi.bitcast(F32), ALU.subtract).then_inc(w_ready, 1)

            def late_weights():
                dve.wait_ge(late_weights_in, 16 * 2)
                for e in range(E):
                    raw = ew_raw[:, e].rearrange("p (c t) -> p c t", t=TAPS)[:, :, CENTER]
                    fold(KC + e, raw, 1 + e)
                for j in range(CO):
                    fold(KC + E + j, w3_raw[:, j], 1 + E + j)
                for m in range(KC, KC + E + CO):
                    split_weights(m + 1, m)

            all_pairs = [P, BLOCKS, E, E]

            def gate(i, o, n, turn):
                if not exists(n) or turn >= len(GATE_TURNS[o % 2]):
                    return
                name = GATE_TURNS[o % 2][turn]
                if name == "turned_logits":
                    dve.wait_ge(router_done, count(i, o + 1, 1, 1))
                    nc.vector.transpose(turned_logits[:, :, :].rearrange("p b c -> p (b c)"), ps_logits[:, 0:HALF])\
                        .then_inc(gate_step, 1)
                elif name == "diff":
                    dve.wait_ge(logits_copied, pairs(i, o, 1, 1))
                    nc.vector.tensor_tensor(
                        diff, logits_copy.unsqueeze(2).broadcast_to(all_pairs),
                        logits[:, :, :].unsqueeze(3).broadcast_to(all_pairs), ALU.subtract).then_inc(gate_step, 1)
                elif name == "beats":
                    dve.wait_ge(gate_step, made(i, o, "diff"))
                    nc.vector.tensor_tensor(
                        beats, diff, tie[:, :, :].unsqueeze(1).broadcast_to(all_pairs),
                        ALU.is_gt).then_inc(gate_step, 1)
                elif name == "rank":
                    dve.wait_ge(gate_step, made(i, o, "beats"))
                    nc.vector.tensor_reduce(rank, beats, AX_X, ALU.add).then_inc(gate_step, 1)
                elif name == "top":
                    dve.wait_ge(side_step, side_made(i, o, "logits"))
                    nc.vector.tensor_reduce(top[:, :], logits[:, :, :], AX_X, ALU.max).then_inc(gate_step, 1)
                elif name == "second_logit":
                    dve.wait_ge(gate_step, made(i, o, "rank"))
                    dve.wait_ge(sign_made, pairs(i, o, 1, 1))
                    nc.vector.scalar_tensor_tensor(
                        second_logit[:, :, :], rank, 1.0, logits[:, :, :], ALU.is_equal,
                        ALU.mult).then_inc(gate_step, 1)
                elif name == "second":
                    dve.wait_ge(gate_step, made(i, o, "second_logit"))
                    nc.vector.tensor_reduce(second, second_logit[:, :, :], AX_X, ALU.add).then_inc(gate_step, 1)
                elif name == "gap":
                    dve.wait_ge(gate_step, made(i, o, "second"))
                    nc.vector.tensor_tensor(gap[:, :], top[:, :], second, ALU.subtract).then_inc(gate_step, 1)
                elif name == "weight":
                    dve.wait_ge(side_step, side_made(i, o, "half_more"))
                    nc.vector.scalar_tensor_tensor(
                        weight, rank, 2.0, half_more[:, :, :], ALU.is_lt,
                        ALU.mult).then_inc(gate_step, 1)
                elif name == "rest":
                    dve.wait_ge(gate_step, made(i, o, "weight"))
                    dve.wait_ge(part_made, pairs(i, o, 2, 1))
                    nc.vector.tensor_tensor(rest, weight, parts[:, :, :, 0],
                                            ALU.subtract).then_inc(gate_step, 1)
                elif name == "low":
                    dve.wait_ge(gate_step, made(i, o, "rest"))
                    dve.wait_ge(part_made, pairs(i, o, 2, 2))
                    nc.vector.tensor_tensor(parts[:, :, :, 2], rest, parts[:, :, :, 1],
                                            ALU.subtract).then_inc(gate_step, 1)
                elif name == "turned_gates":
                    dve.wait_ge(gate_step, made(i, o, "low"))
                    nc.vector.transpose(gates_T[:, o // 2 % PAIRS], gate_parts[:, :, :].rearrange("p b c -> p (b c)"))\
                        .then_inc(gate_step, 1)

            def low_tokens(i, o, n):
                if exists(n):
                    dve.wait_ge(tok_hi_made, count(i, o, 1, 1))
                    nc.vector.tensor_tensor(tok_lo[:, o % TOK_SLOTS], ps_tok[:, :],
                                            tok_hi[:, o % TOK_SLOTS].bitcast(F32), ALU.subtract)\
                        .then_inc(tok_lo_made, 1)

            def mul(i, o, n, e):
                if exists(n):
                    dve.wait_ge(y_made, count(i, o, E, e + 1))
                    dve.wait_ge(gate_spread, count(i, o, E, e + 1))
                    where = acc[:, 0] if e == 0 else ps_gate[:, bank(o, e)]
                    nc.vector.tensor_tensor(where, y[:, e], ps_gate[:, bank(o, e)], ALU.mult).then_inc(mix_step, 1)

            def add(i, o, n, e):
                if exists(n):
                    dve.wait_ge(mix_step, count(i, o, MIX_STEPS, MIX_NEEDS[e]))
                    where = acc[:, e] if e < E - 1 else ps_gate[:, bank(o, e)]
                    nc.vector.tensor_tensor(where, ps_gate[:, bank(o, e)], acc[:, e - 1], ALU.add).then_inc(mix_step, 1)

            def low_mix(i, o, n):
                if exists(n):
                    dve.wait_ge(mix_hi_made, count(i, o, 1, 1))
                    nc.vector.tensor_tensor(mix_lo[:, o % 2], ps_gate[:, bank(o, E - 1)], mix_hi[:, o % 2].bitcast(F32),
                                            ALU.subtract).then_inc(mix_lo_made, 1)

            def lead_in(i, o, n):
                def at(by):
                    return shifted(i, o, n, by)

                if n == LATE_WEIGHTS_AT:
                    late_weights()
                gate(*at(2), 0)
                gate(*at(2), 1)
                gate(*at(2), 2)
                gate(*at(2), 3)
                gate(*at(2), 4)
                gate(*at(2), 5)
                low_tokens(*at(4))

            def step(i, o, n):
                def at(by):
                    return shifted(i, o, n, by)

                mul(*at(0), 0)
                gate(*at(2), 0)
                low_mix(*at(-1))
                mul(*at(0), 1)
                gate(*at(2), 1)
                add(*at(0), 1)
                mul(*at(0), 2)
                gate(*at(2), 2)
                add(*at(0), 2)
                gate(*at(2), 3)
                mul(*at(0), 3)
                gate(*at(2), 4)
                gate(*at(2), 5)
                low_tokens(*at(4))
                add(*at(0), 3)

            run_steps(dve, step, lead_in)

        @block.tensor
        def _(pe):
            def turn_weights(t, m):
                pe.wait_ge(w_folded, m + 1)
                if t >= 2:
                    pe.wait_ge(w_ready, t - 1)
                nc.tensor.transpose(ps_y[:, t % 2, 0:P], w_scaled[:, m], ident[:, :]).then_inc(w_turned, 1)

            pe.wait_ge(consts_made, 11)
            for k in range(KC):
                turn_weights(k, k)
            t = ROUTER_TURN
            pe.wait_ge(params_in, 16 * PARAMS)
            pe.wait_ge(w_ready, t - 1)
            nc.tensor.transpose(ps_y[:, t % 2, 0:E], rw_raw[:, :], ident[0:E, 0:E]).then_inc(w_turned, 1)
            pe.wait_ge(w_ready, t + 1)

            def late_weights():
                for m in range(KC, KC + E + CO):
                    turn_weights(m + 1, m)
                pe.wait_ge(w_ready, KC + E + CO + 1)

            def product(where, m0, hi, lo):
                terms = []
                for k in range(len(hi)):
                    terms += [(wT_hi[:, m0 + k], hi[k]), (wT_lo[:, m0 + k], hi[k]), (wT_hi[:, m0 + k], lo[k])]
                for t, (w, v) in enumerate(terms):
                    last = nc.tensor.matmul(where, w, v, start=(t == 0), stop=(t == len(terms) - 1))
                return last

            def conv(i, o, n):
                if exists(n):
                    pe.wait_ge(x_lo_made, count(i, o, 1, 1))
                    if has_before(n, 1):
                        pe.wait_ge(tok_lo_made, count(i, o - 1, 1, 1))
                    product(ps_tok[:, :], 0, [x_hi[:, o % 2, k] for k in range(KC)],
                            [x_lo[:, o % 2, k] for k in range(KC)]).then_inc(conv_done, 1)

            def router(i, o, n):
                if exists(n):
                    pe.wait_ge(tok_lo_made, count(i, o, 1, 1))
                    if o % 2 == 0 and has_before(n, 2):
                        pe.wait_ge(gate_step, made(i, o - 2, "turned_logits"))
                    for part in range(2):
                        q = o % 2 * 2 + part
                        tokens = slice(part * HALF, (part + 1) * HALF)
                        weights = slice(q * P, (q + 1) * P)
                        nc.tensor.matmul(ps_logits[:, 0:HALF], router_both[:, weights],
                                         tok_hi[:, o % TOK_SLOTS, tokens], start=(q == 0), stop=False)
                        last = nc.tensor.matmul(ps_logits[:, 0:HALF], router_hi[:, weights],
                                                tok_lo[:, o % TOK_SLOTS, tokens], start=False,
                                                stop=(q == QUARTERS - 1))
                    last.then_inc(router_done, 1)

            def expert(i, o, n, e):
                if exists(n):
                    if e >= 2 or has_before(n, 1):
                        pe.wait_ge(y_made, count(i, o, E, e - 1))
                    product(ps_y[:, e % 2], KC + e, [tok_hi[:, o % TOK_SLOTS]], [tok_lo[:, o % TOK_SLOTS]])\
                        .then_inc(expert_done, 1)

            def spread(i, o, n, e):
                if exists(n):
                    if e == 0:
                        pe.wait_ge(gate_step, made(i, o, "turned_gates"))
                    if e == 0 and has_before(n, 1):
                        pe.wait_ge(mix_step, count(i, o - 1, MIX_STEPS, MIX_ADD[2]))
                    if e == 1:
                        pe.wait_ge(mix_step, count(i, o, MIX_STEPS, MIX_MUL[0]))
                    if e == 2 and has_before(n, 1):
                        pe.wait_ge(mix_lo_made, count(i, o - 1, 1, 1))
                    if e == 3:
                        pe.wait_ge(mix_step, count(i, o, MIX_STEPS, MIX_ADD[1]))
                    for part in range(2):
                        last = nc.tensor.matmul(ps_gate[:, bank(o, e), part * HALF:(part + 1) * HALF],
                                                select[:, (o % 2 * 2 + part) * E + e],
                                                gates_T[:, o // 2 % PAIRS], start=True, stop=True)
                    last.then_inc(gate_spread, 1)

            def output(i, o, n, j):
                if exists(n):
                    pe.wait_ge(mix_lo_made, count(i, o, 1, 1))
                    if j > 0:
                        pe.wait_ge(out_silu[j - 1], count(i, o, 1, 1))
                    elif has_before(n, 1):
                        pe.wait_ge(out_silu[CO - 1], count(i, o - 1, 1, 1))
                    product(ps_out[:, :], KC + E + j, [mix_hi[:, o % 2]], [mix_lo[:, o % 2]]).then_inc(out_done[j], 1)

            def lead_in(i, o, n):
                def at(by):
                    return shifted(i, o, n, by)

                router(*at(3))
                conv(*at(4))
                if n == LATE_WEIGHTS_AT:
                    late_weights()

            def step(i, o, n):
                def at(by):
                    return shifted(i, o, n, by)

                expert(*at(0), 0)
                expert(*at(0), 1)
                output(*at(-2), 0)
                spread(*at(0), 0)
                expert(*at(0), 2)
                router(*at(3))
                expert(*at(0), 3)
                spread(*at(0), 1)
                output(*at(-2), 1)
                spread(*at(0), 2)
                conv(*at(4))
                spread(*at(0), 3)

            run_steps(pe, step, lead_in)


_INS = ["x", "L0_conv_w1", "L0_conv_bn1_g", "L0_conv_bn1_b", "L0_conv_bn1_m", "L0_conv_bn1_v",
        "L0_conv_router_w", "L0_conv_router_b", "L0_conv_ew", "L0_conv_ebn_g", "L0_conv_ebn_b",
        "L0_conv_ebn_m", "L0_conv_ebn_v", "L0_conv_w3", "L0_conv_bn3_g", "L0_conv_bn3_b",
        "L0_conv_bn3_m", "L0_conv_bn3_v"]


def kernel(**inputs):
    import numpy as _np
    import concourse.bacc as _bacc
    from concourse import mybir as _mybir
    from concourse.bass_utils import run_bass_kernel_spmd as _run

    nc = _bacc.Bacc("TRN2", target_bir_lowering=False, num_devices=1)
    arrays, args = {}, []
    for name in _INS:
        a = _np.ascontiguousarray(inputs[name])
        arrays[f"in_{name}_dram"] = a
        args.append(nc.dram_tensor(f"in_{name}_dram", a.shape, _mybir.dt.from_np(a.dtype), kind="ExternalInput").ap())
    shape = inputs["x"].shape
    args.append(nc.dram_tensor("out_0_dram", shape, _mybir.dt.float32, kind="ExternalOutput").ap())
    moe_conv_kernel(nc, *args)
    r = _run(nc, [arrays], core_ids=[0])
    return r.results[0]["out_0_dram"]
```
